# Optimizing a Trainium2 kernel written in Bass

```python
import numpy as np
import jax
import jax.numpy as jnp

def _softmax(x, axis=-1):
    return jax.nn.softmax(x, axis=axis)

def _gelu(x):
    return jax.nn.gelu(x, approximate=True)

def _silu(x):
    return jax.nn.silu(x)

def _sigmoid(x):
    return jax.nn.sigmoid(x)

def _layernorm(x, axis=-1, eps=1e-05):
    m = jnp.mean(x, axis=axis, keepdims=True)
    v = jnp.var(x, axis=axis, keepdims=True)
    return (x - m) / jnp.sqrt(v + eps)

def _scatter_add(tgt, idx, src, axis=0):
    return tgt.at[idx].add(src)

def _segment_sum(src, seg, n):
    return jax.ops.segment_sum(src, seg, n)
kernel_name = 'mk_adj_ffn_d2_adj_r2_e56d70'

def setup_inputs(seed: int=0):
    np.random.seed(seed)
    _w = jnp.asarray

    def _rec_inputs():
        import jax
        import jax.numpy as jnp
        _gk = jax.random.key(seed)
        x = -8.015e-05 + 0.9999 * jax.random.normal(jax.random.fold_in(_gk, 1), (32, 256, 128), jnp.float32)
        _a = jax.random.bernoulli(jax.random.fold_in(_gk, 2), 0.015625, (32, 256, 256))
        _a = jnp.logical_or(_a, jnp.swapaxes(_a, -1, -2))
        _a = jnp.logical_or(_a, jnp.eye(256, dtype=bool))
        _af = _a.astype(jnp.float32)
        _af = _af * jax.random.uniform(jax.random.fold_in(_gk, 3), (32, 256, 256), jnp.float32, 0.05, 0.999837)
        adj = _af
        return (x, adj)
    x, adj = _rec_inputs()

    def _L0_gnn_setup():
        import jax, jax.numpy as jnp
        import numpy as np
        GROUPS = [list(range(25)), [0, 1, 2, 3, 4, 5, 6, 7, 8], [0, 9, 10, 11, 12, 13, 14], [6, 7, 8, 12, 13, 14], [3, 4, 5, 9, 10, 11]]
        B, N, D_IN, D_HID = (4096, 25, 128, 256)

        def _graph_conv(x, adj, W, b):
            n = adj.shape[-1]
            A = adj + jnp.eye(n, dtype=adj.dtype)
            deg = jnp.sum(A, axis=-1)
            deg_safe = jnp.where(deg == 0, 1.0, deg)
            dinv = jnp.where(deg == 0, 0.0, deg_safe ** (-0.5))
            norm_adj = dinv[:, :, None] * A * dinv[:, None, :]
            support = jnp.einsum('bnd,de->bne', x, W)
            out = jnp.einsum('bnm,bme->bne', norm_adj, support) + b
            return jax.nn.relu(out)
        key = jax.random.key(seed)
        ks = jax.random.split(key, 7)
        s1 = float(np.sqrt(6.0 / (D_IN + D_HID)))
        s2 = float(np.sqrt(6.0 / (D_HID + D_IN)))
        return {'x': jax.random.normal(ks[0], (B, N, D_IN), dtype=jnp.float32), 'adj': jax.random.uniform(ks[1], (B, N, N), dtype=jnp.float32), 'W1': jax.random.uniform(ks[2], (5, D_IN, D_HID), jnp.float32, -s1, s1), 'b1': jnp.zeros((5, D_HID), dtype=jnp.float32), 'W2': jax.random.uniform(ks[3], (5, D_HID, D_IN), jnp.float32, -s2, s2), 'b2': jnp.zeros((5, D_IN), dtype=jnp.float32), 'fusion_w': jnp.ones((5,), dtype=jnp.float32)}
    _L0_gnn_all = _L0_gnn_setup()
    _L0_gnn_in = {k: v for k, v in _L0_gnn_all.items() if k in ('W1', 'b1', 'W2', 'b2', 'fusion_w')}
    del _L0_gnn_all

    def _L0_ffn_setup():
        import jax, jax.numpy as jnp
        import numpy as np
        from jax import lax
        key = jax.random.key(seed)
        B, T, I, H = (64, 1024, 128, 128)
        ks = jax.random.split(key, 13)
        s = 1.0 / np.sqrt(H)

        def w(k, shape):
            return jax.random.uniform(k, shape, jnp.float32, -s, s)
        return {'x': jax.random.normal(ks[0], (B, T, I), jnp.float32), 'U_i': w(ks[1], (I, H)), 'V_i': w(ks[2], (H, H)), 'b_i': w(ks[3], (H,)), 'U_f': w(ks[4], (I, H)), 'V_f': w(ks[5], (H, H)), 'b_f': w(ks[6], (H,)), 'U_c': w(ks[7], (I, H)), 'V_c': w(ks[8], (H, H)), 'b_c': w(ks[9], (H,)), 'U_o': w(ks[10], (I, H)), 'V_o': w(ks[11], (H, H)), 'b_o': w(ks[12], (H,))}
    _L0_ffn_all = _L0_ffn_setup()
    _L0_ffn_in = {k: v for k, v in _L0_ffn_all.items() if k in ('U_i', 'V_i', 'b_i', 'U_f', 'V_f', 'b_f', 'U_c', 'V_c', 'b_c', 'U_o', 'V_o', 'b_o')}
    del _L0_ffn_all

    def _L1_gnn_setup():
        import jax, jax.numpy as jnp
        import numpy as np
        MIN_VALUE = 1e-10
        key = jax.random.key(seed)
        k1, k2, k3, k4, k5 = jax.random.split(key, 5)
        B, N, F, P = (32, 512, 128, 128)
        x = jax.random.normal(k1, (B, N, F), dtype=jnp.float32)
        adjacency_matrix = jax.random.uniform(k2, (B, N, N), dtype=jnp.float32)
        bound = 1.0 / np.sqrt(F)
        W = jax.random.uniform(k3, (P, F), minval=-bound, maxval=bound, dtype=jnp.float32)
        b = jax.random.uniform(k4, (P,), minval=-bound, maxval=bound, dtype=jnp.float32)
        alpha = jax.random.uniform(k5, (1,), dtype=jnp.float32)
        return {'x': x, 'adjacency_matrix': adjacency_matrix, 'W': W, 'b': b, 'alpha': alpha}
    _L1_gnn_all = _L1_gnn_setup()
    _L1_gnn_in = {k: v for k, v in _L1_gnn_all.items() if k in ('W', 'b', 'alpha')}
    del _L1_gnn_all

    def _L1_ffn_setup():
        import jax, jax.numpy as jnp
        import numpy as np
        E = 8
        K = 2
        D = 128
        H = 256
        DOUT = 128
        EPS = 1e-05
        key = jax.random.key(seed)
        ks = jax.random.split(key, 9)
        s = 0.02
        return {'x': jax.random.normal(ks[0], (4, 4096, D), jnp.float32), 'gamma': 1.0 + 0.05 * jax.random.normal(ks[1], (D,), jnp.float32), 'beta': 0.05 * jax.random.normal(ks[2], (D,), jnp.float32), 'Wr': 0.01 * jax.random.normal(ks[3], (D, E), jnp.float32), 'br': jnp.zeros((E,), jnp.float32), 'W1': s * jax.random.normal(ks[4], (E, D, H), jnp.float32), 'b1': s * jax.random.normal(ks[5], (E, H), jnp.float32), 'W2': s * jax.random.normal(ks[6], (E, H, DOUT), jnp.float32), 'b2': s * jax.random.normal(ks[7], (E, DOUT), jnp.float32)}
    _L1_ffn_all = _L1_ffn_setup()
    _L1_ffn_in = {k: v for k, v in _L1_ffn_all.items() if k in ('gamma', 'beta', 'Wr', 'br', 'W1', 'b1', 'W2', 'b2')}
    del _L1_ffn_all
    return {'x': x, 'adj': adj, 'L0_gnn_W1': _L0_gnn_in['W1'], 'L0_gnn_b1': _L0_gnn_in['b1'], 'L0_gnn_W2': _L0_gnn_in['W2'], 'L0_gnn_b2': _L0_gnn_in['b2'], 'L0_gnn_fusion_w': _L0_gnn_in['fusion_w'], 'L0_ffn_U_i': _L0_ffn_in['U_i'], 'L0_ffn_V_i': _L0_ffn_in['V_i'], 'L0_ffn_b_i': _L0_ffn_in['b_i'], 'L0_ffn_U_f': _L0_ffn_in['U_f'], 'L0_ffn_V_f': _L0_ffn_in['V_f'], 'L0_ffn_b_f': _L0_ffn_in['b_f'], 'L0_ffn_U_c': _L0_ffn_in['U_c'], 'L0_ffn_V_c': _L0_ffn_in['V_c'], 'L0_ffn_b_c': _L0_ffn_in['b_c'], 'L0_ffn_U_o': _L0_ffn_in['U_o'], 'L0_ffn_V_o': _L0_ffn_in['V_o'], 'L0_ffn_b_o': _L0_ffn_in['b_o'], 'L1_gnn_W': _L1_gnn_in['W'], 'L1_gnn_b': _L1_gnn_in['b'], 'L1_gnn_alpha': _L1_gnn_in['alpha'], 'L1_ffn_gamma': _L1_ffn_in['gamma'], 'L1_ffn_beta': _L1_ffn_in['beta'], 'L1_ffn_Wr': _L1_ffn_in['Wr'], 'L1_ffn_br': _L1_ffn_in['br'], 'L1_ffn_W1': _L1_ffn_in['W1'], 'L1_ffn_b1': _L1_ffn_in['b1'], 'L1_ffn_W2': _L1_ffn_in['W2'], 'L1_ffn_b2': _L1_ffn_in['b2']}

def reference(x, adj, L0_gnn_W1, L0_gnn_b1, L0_gnn_W2, L0_gnn_b2, L0_gnn_fusion_w, L0_ffn_U_i, L0_ffn_V_i, L0_ffn_b_i, L0_ffn_U_f, L0_ffn_V_f, L0_ffn_b_f, L0_ffn_U_c, L0_ffn_V_c, L0_ffn_b_c, L0_ffn_U_o, L0_ffn_V_o, L0_ffn_b_o, L1_gnn_W, L1_gnn_b, L1_gnn_alpha, L1_ffn_gamma, L1_ffn_beta, L1_ffn_Wr, L1_ffn_br, L1_ffn_W1, L1_ffn_b1, L1_ffn_W2, L1_ffn_b2):
    import jax
    import jax.numpy as jnp

    def _L0_gnn_ref(x, adj, W1, b1, W2, b2, fusion_w):
        import jax, jax.numpy as jnp
        import numpy as np
        GROUPS = [list(range(25)), [0, 1, 2, 3, 4, 5, 6, 7, 8], [0, 9, 10, 11, 12, 13, 14], [6, 7, 8, 12, 13, 14], [3, 4, 5, 9, 10, 11]]
        B, N, D_IN, D_HID = (4096, 25, 128, 256)

        def _graph_conv(x, adj, W, b):
            n = adj.shape[-1]
            A = adj + jnp.eye(n, dtype=adj.dtype)
            deg = jnp.sum(A, axis=-1)
            deg_safe = jnp.where(deg == 0, 1.0, deg)
            dinv = jnp.where(deg == 0, 0.0, deg_safe ** (-0.5))
            norm_adj = dinv[:, :, None] * A * dinv[:, None, :]
            support = jnp.einsum('bnd,de->bne', x, W)
            out = jnp.einsum('bnm,bme->bne', norm_adj, support) + b
            return jax.nn.relu(out)
        norm_w = jax.nn.softmax(fusion_w)
        fused = jnp.zeros_like(x)
        for g, idx_list in enumerate(GROUPS):
            idx = jnp.asarray(idx_list)
            x_g = x[:, idx, :]
            adj_g = adj[:, idx][:, :, idx]
            h = _graph_conv(x_g, adj_g, W1[g], b1[g])
            out_g = _graph_conv(h, adj_g, W2[g], b2[g])
            fused = fused.at[:, idx, :].add(norm_w[g] * out_g)
        return fused

    def _L0_ffn_ref(x, U_i, V_i, b_i, U_f, V_f, b_f, U_c, V_c, b_c, U_o, V_o, b_o):
        import jax, jax.numpy as jnp
        import numpy as np
        from jax import lax
        B, T, _ = x.shape
        H = U_i.shape[1]
        xt = jnp.swapaxes(x, 0, 1)
        xi = xt @ U_i + b_i
        xf = xt @ U_f + b_f
        xg = xt @ U_c + b_c
        xo = xt @ U_o + b_o
        h0 = jnp.zeros((B, H), x.dtype)
        c0 = jnp.zeros((B, H), x.dtype)

        def step(carry, xs):
            h, c = carry
            xi_t, xf_t, xg_t, xo_t = xs
            i_t = jax.nn.sigmoid(xi_t + h @ V_i)
            f_t = jax.nn.sigmoid(xf_t + h @ V_f)
            g_t = jnp.tanh(xg_t + h @ V_c)
            o_t = jax.nn.sigmoid(xo_t + h @ V_o)
            c_new = h * c + i_t * g_t
            h_new = o_t * jnp.tanh(c_new)
            return ((h_new, c_new), h_new)
        (_, _), hs = lax.scan(step, (h0, c0), (xi, xf, xg, xo))
        return jnp.swapaxes(hs, 0, 1)

    def _L1_gnn_ref(x, adjacency_matrix, W, b, alpha):
        import jax, jax.numpy as jnp
        import numpy as np
        MIN_VALUE = 1e-10
        deg = adjacency_matrix.sum(axis=-1)
        deg = jnp.where(deg != 0, deg, 1.0)
        d_inv_sqrt = deg ** (-0.5)
        norm_adj = d_inv_sqrt[:, :, None] * adjacency_matrix * d_inv_sqrt[:, None, :]
        alpha_eff = jnp.maximum(alpha[0], MIN_VALUE)
        N = adjacency_matrix.shape[1]
        a_plus = norm_adj + alpha_eff * jnp.eye(N, dtype=adjacency_matrix.dtype)
        h = jnp.einsum('bnm,bmf->bnf', a_plus, x)
        return jnp.einsum('bnf,pf->bnp', h, W) + b

    def _L1_ffn_ref(x, gamma, beta, Wr, br, W1, b1, W2, b2):
        import jax, jax.numpy as jnp
        import numpy as np
        E = 8
        K = 2
        D = 128
        H = 256
        DOUT = 128
        EPS = 1e-05
        mu = jnp.mean(x, axis=-1, keepdims=True)
        var = jnp.mean(jnp.square(x - mu), axis=-1, keepdims=True)
        xn = (x - mu) * jax.lax.rsqrt(var + EPS) * gamma + beta
        logits = jnp.einsum('bsd,de->bse', xn, Wr) + br
        top_vals, top_idx = jax.lax.top_k(logits, K)
        w = jax.nn.softmax(top_vals, axis=-1)
        w_full = jnp.einsum('bsk,bske->bse', w, jax.nn.one_hot(top_idx, E, dtype=w.dtype))
        y = jnp.zeros(x.shape[:-1] + (DOUT,), x.dtype)
        for e in range(E):
            h = jax.nn.gelu(jnp.einsum('bsd,dh->bsh', xn, W1[e]) + b1[e], approximate=False)
            y_e = jnp.einsum('bsh,hd->bsd', h, W2[e]) + b2[e]
            y = y + y_e * w_full[..., e, None]
        return y
    x = x + _L0_gnn_ref(_layernorm(x, axis=-1), adj, L0_gnn_W1, L0_gnn_b1, L0_gnn_W2, L0_gnn_b2, L0_gnn_fusion_w)
    x = x + _L0_ffn_ref(_layernorm(x, axis=-1), L0_ffn_U_i, L0_ffn_V_i, L0_ffn_b_i, L0_ffn_U_f, L0_ffn_V_f, L0_ffn_b_f, L0_ffn_U_c, L0_ffn_V_c, L0_ffn_b_c, L0_ffn_U_o, L0_ffn_V_o, L0_ffn_b_o)
    x = x + _L1_gnn_ref(_layernorm(x, axis=-1), adj, L1_gnn_W, L1_gnn_b, L1_gnn_alpha)
    x = x + _L1_ffn_ref(_layernorm(x, axis=-1), L1_ffn_gamma, L1_ffn_beta, L1_ffn_Wr, L1_ffn_br, L1_ffn_W1, L1_ffn_b1, L1_ffn_W2, L1_ffn_b2)
    return x

_drawn_inputs = setup_inputs


def setup_inputs(seed=0):
    import zlib

    import numpy as np

    out = dict(_drawn_inputs(seed))
    spreads = {'L0_gnn_b1': (0.0, 0.8),
     'L0_gnn_b2': (0.0, 0.8),
     'L0_gnn_fusion_w': (1.0, 0.6),
     'L1_ffn_br': (0.0, 0.34)}
    factors = {'L0_ffn_V_i': 8.0,
     'L0_ffn_b_i': 8.0,
     'L0_ffn_V_c': 3.754,
     'L0_ffn_b_c': 4.171,
     'L0_ffn_V_o': 8.0,
     'L0_ffn_b_o': 8.0,
     'L1_ffn_gamma': 8.0,
     'L1_ffn_beta': 8.0,
     'L1_ffn_b1': 8.0,
     'L1_ffn_b2': 4.301}
    for name, (base, spread) in spreads.items():
        noise = np.random.default_rng([zlib.crc32(name.encode()), seed]).standard_normal(out[name].shape)
        drawn = base * np.exp(spread * noise) if base else spread * noise
        out[name] = jnp.asarray(drawn.astype(out[name].dtype))
    for name, factor in factors.items():
        out[name] = (out[name] * factor).astype(out[name].dtype)
    return out
```

```python
from contextlib import ExitStack

import concourse.bass as bass
from concourse import mybir

F32 = mybir.dt.float32
F32R = mybir.dt.float32r
BF16 = mybir.dt.bfloat16
F16 = mybir.dt.float16
U32 = mybir.dt.uint32
ALU = mybir.AluOpType
ACT = mybir.ActivationFunctionType
AXX = mybir.AxisListType.X

P = 128
B, T, D = 32, 256, 128
HID = 256
E = 8
GROUPS = [list(range(25)), [0, 1, 2, 3, 4, 5, 6, 7, 8], [0, 9, 10, 11, 12, 13, 14],
          [6, 7, 8, 12, 13, 14], [3, 4, 5, 9, 10, 11]]
NG = len(GROUPS)
NN = 25
OFF = [sum(len(g) for g in GROUPS[:i]) for i in range(NG + 1)]
NP = OFF[-1]
NTILE = -(-NN * B // P)
TT = P // B
STEPS = 8
NGRP = T // STEPS
XPAD = 2
NX = XPAD + T // TT + 4
LN_EPS = 1e-5
SC = 1024.0
LAG = 3
NB2 = B // 2

C_ID = 0
C_SEL = C_ID + P
C_M5 = C_SEL + NP
C_MASK = C_M5 + NG
C_IOTA = C_MASK + 2 * NP
C_ONES = C_IOTA + E
C_SELE = C_ONES + P
C_N = C_SELE + E * P


def runs(nodes):
    out = []
    for j, n in enumerate(nodes):
        if out and out[-1][1] + out[-1][2] == n:
            out[-1][2] += 1
        else:
            out.append([j, n, 1])
    return [tuple(r) for r in out]


RUNS = [(g, j, n, k) for g in range(NG) for j, n, k in runs(GROUPS[g])]
HCHUNKS = [(0, 0, 16), (0, 16, 32)] + [(g, 0, 32) for g in range(1, NG)]


def build(nc, io):
    x_in, adj_in, out = io["x"], io["adj"], io["out"]

    with ExitStack() as ctx:
        def sb(name, shape, dt=F32, where=None):
            return (where or ctx).enter_context(nc.sbuf_tensor(name, shape, dt))

        def psum(name, shape, dt=F32, where=None):
            return (where or ctx).enter_context(nc.psum_tensor(name, shape, dt))

        def sem(name):
            return ctx.enter_context(nc.semaphore(name))

        ln_nodes_d = nc.dram_tensor("ln_nodes_d", (NTILE * P, D), F32, kind="Internal").ap()
        x2_d = nc.dram_tensor("x2_d", ((NGRP + 1) * STEPS * B, D), F32, kind="Internal").ap()
        y_d = nc.dram_tensor("y_d", ((NGRP + 1) * STEPS * B, D), F32, kind="Internal").ap()

        const = sb("const", [P, C_N])
        ident = const[:, C_ID:C_ID + P]
        ones = const[:, C_ONES:C_ONES + P]
        iota8 = const[:, C_IOTA:C_IOTA + E]
        adjT = sb("adjT", [P, B, 2, T])
        w1hi, w1lo = sb("w1hi", [P, E, HID], F32R), sb("w1lo", [P, E, HID], F32R)
        w2hi, w2lo = sb("w2hi", [P, E, 2, D], F32R), sb("w2lo", [P, E, 2, D], F32R)
        gnn_wT = sb("gnn_wT", [P, D])
        wr = sb("wr", [P, E])
        br = sb("br", [P, E])
        NV = 2 * NG + NG + 2 + 2 * E
        vcols = sb("vcols", [P, NV])
        ab1 = vcols[:, 0:2 * NG].rearrange("p (g c) -> p g c", c=2)
        ab2 = vcols[:, 2 * NG:3 * NG]
        gamma, beta = vcols[:, 3 * NG:3 * NG + 1], vcols[:, 3 * NG + 1:3 * NG + 2]
        eb1 = vcols[:, 3 * NG + 2:].rearrange("p (e c) -> p e c", c=2)
        b2p = sb("b2p", [3 * E, 3, D], BF16)
        brow = sb("brow", [3, 4, P], BF16)
        ones3 = sb("ones3", [3, 2 * P], BF16)
        sel_e = sb("sel_e", [3 * E, E, P], BF16)
        identb = sb("identb", [P, P], BF16)
        alpha = sb("alpha", [P, 1])

        ld_x, ld_adj25, ld_const, ld_wa, ld_wb, ld_small, ld_lstm = (sem(n) for n in (
            "ld_x", "ld_adj25", "ld_const", "ld_wa", "ld_wb", "ld_small", "ld_lstm"))
        chain = sem("dve_chain")
        chains = [0]

        with ExitStack() as rec:
            X = sb("X", [P, NX, D], where=rec)
            us = sb("us", [P, 3, P], where=rec)
            vp = [sb(f"vp{i}", [P, 3, P], BF16, where=rec) for i in range(3)]
            adjn = [sb(f"adjn{i}", [P, 2, T], where=rec) for i in range(2)]
            adjs = sb("adjs", [P, 2, T], where=rec)
            junk = sb("junk", [P, T], where=rec)
            S = sb("S", [P, 2, B, 2], where=rec)
            GC = sb("GC", [P, B, 2], where=rec)
            CC = sb("CC", [P, B, 2], where=rec)
            tanh_c = sb("tanh_c", [P, B], where=rec)
            h1, h2 = sb("h1", [P, B], F16, where=rec), sb("h2", [P, B], F16, where=rec)
            hs = [sb(f"hs{i}", [P, STEPS * B], where=rec) for i in range(2)]
            xn = sb("xn", [P, 2, D], where=rec)
            xbuf = sb("xbuf", [P, STEPS * B], where=rec)
            x2s, ys = sb("x2s", [P, 2, D], where=rec), sb("ys", [P, 2, D], where=rec)
            st_x, mv_x, rs_x = sb("st_x", [P, 2, 6], where=rec), sb("mv_x", [P, 2, 2], where=rec), sb("rs_x", [P, 2], where=rec)
            st_y, mv_y, rs_y = sb("st_y", [P, 2, 6], where=rec), sb("mv_y", [P, 2, 2], where=rec), sb("rs_y", [P, 2], where=rec)
            ve_x, ve_y = sb("ve_x", [P, 2], where=rec), sb("ve_y", [P, 2], where=rec)
            eps2, mhalf = sb("eps2", [P, 2], where=rec), sb("mhalf", [P, 2], where=rec)
            tick = sb("tick", [P, 2], where=rec)
            deg, degs, dinv, sdiag = (sb(n, [P, 2], where=rec) for n in ("deg", "degs", "dinv", "sdiag"))

            pre = ExitStack()
            V = sb("V", [P, 3, P], where=pre)
            U = sb("U", [P, 3, P], where=pre)
            Vr = sb("Vr", [P, 3, P], where=pre)
            wst = sb("wst", [P, E * HID], where=pre)
            w2st = sb("w2st", [P, E, 2, D], where=pre)
            gw = sb("gw", [P, D], where=pre)
            bst = sb("bst", [3, 4, P], where=pre)
            bpa = [sb(f"bpa{i}", [3, 4, P], BF16, where=pre) for i in range(3)]
            bra = sb("bra", [3, 4, P], where=pre)
            b2st, b2ra, b2rb = (sb(n, [3 * E, D], where=pre) for n in ("b2st", "b2ra", "b2rb"))
            aW1, aW2 = sb("aW1", [P, NG, HID], where=pre), sb("aW2", [P, NG, 2, D], where=pre)
            vrows = sb("vrows", [NV, P], where=pre)
            fw, fmax, fe, fs, fr, gwt, gb2 = (sb(n, [P, s], where=pre) for n, s in (
                ("fw", NG), ("fmax", 1), ("fe", NG), ("fs", 1), ("fr", 1), ("gwt", NG), ("gb2", NG)))
            st_a, mv_a, rs_a = sb("st_a", [P, NTILE, 6], where=pre), sb("mv_a", [P, NTILE, 2], where=pre), sb("rs_a", [P, NTILE], where=pre)
            lnx = sb("lnx", [P, NTILE, D], where=pre)
            arena, used = adjT[:].rearrange("p b c n -> p (b c n)"), [0]

            def carve(parts, *shape):
                n = 1
                for k in shape:
                    n *= k
                a = arena[0:parts, used[0]:used[0] + n]
                used[0] += n
                names = "abc"[:len(shape)]
                return a.rearrange(f"p ({' '.join(names)}) -> p {' '.join(names)}", **dict(zip(names[1:], shape[1:])))

            XA = carve(NN, B, D)
            adj25 = sb("adj25", [NN, B, NN], where=pre)
            A1 = adj25
            Dbc = carve(P, B, NP)
            Z = carve(P, B, NP)
            Hh = carve(P, 2, B, NP)
            St = carve(P, B, NP)
            Sp = carve(2 * NP, B // 2, D)
            Bd = carve(2 * NP, B // 2, 2, NP)
            Apk = Hh[0:NN, 0]
            Z2 = St
            R = St[0:NN]
            O = Z
            Dg = Z[0:NN]
            few = Sp[0:NN].rearrange("p q d -> p (q d)")
            dg, dgm, dgs, dgr, dgi = (few[:, i * NG * B:(i + 1) * NG * B].rearrange("p (g b) -> p g b", g=NG) for i in range(5))
            seg = few[:, 5 * NG * B:6 * NG * B].rearrange("p (b k) -> p b k", k=5)
            fused = lnx[:].rearrange("p i (t b) -> p (i t) b", b=B)
            pre.close()

        def pair(name, shape, dt=F32):
            return [sb(f"{name}{i}", shape, dt) for i in range(2)]

        yr, x2r = pair("yr", [P, 2, 2 * D]), pair("x2r", [P, 2, 2 * D])
        hts = sb("hts", [P, 4 * P])
        x3 = pair("x3", [P, 2, 2, D])
        xh = sb("xh", [P, 4, D])
        xnT = sb("xnT", [P, 4 * P])
        xhi, xlo = pair("xhi", [P, 4 * P], F32R), pair("xlo", [P, 4 * P], F32R)
        st_m, mv_m, ve_m, rs_m = (sb(n, s) for n, s in (("st_m", [P, 4, 6]), ("mv_m", [P, 4, 2]), ("ve_m", [P, 4]), ("rs_m", [P, 4])))
        half4, eps4, tick_m = sb("half4", [P, 4]), sb("eps4", [P, 4]), sb("tick_m", [P, 1])
        lg, top = sb("lg", [P, 4, E]), sb("top", [P, 4, E])
        top_i = sb("top_i", [P, 4, E], U32)
        idx = sb("idx", [P, 4, 2])
        dif, th = sb("dif", [P, 4]), sb("th", [P, 4])
        w12 = sb("w12", [P, 4, 2])
        oneh, ohw = sb("oneh", [P, 4, 2, E]), sb("ohw", [P, 4, 2, E])
        wf, wra, wrb = sb("wf", [P, 4, E]), sb("wra", [P, 4, E]), sb("wrb", [P, 4, E])
        wp = sb("wp", [P, 4, 3, E], BF16)
        wT = pair("wT", [3 * E, 4 * P], BF16)
        Gl = pair("Gl", [P, 2, 4 * P])
        Gw = pair("Gw", [P, 2, 4 * P])
        ghi, glo = ([sb(f"{h}{i}", [P, 2, 4 * P], F32R) for i in range(4)] for h in ("ghi", "glo"))
        yTs = sb("yTs", [P, 4 * P])
        outb = pair("outb", [P, 2, 2, D])

        PB = [psum(f"pb{i}", [P, 512]) for i in range(8)]

        (ln_nodes_ready, ln_nodes_stored, XA_loaded, A1_ready, Apk_ready, Dg_ready, adjT25_ps, dbc_ps, gwT_ps, bp_ps,
         R_ready, dbc_sb, gwT_sb, bd_ready, z_ps, z_ready, h_ps, h_act, h_dve, s_ps, s_ready, sp_ps, sp_ready, z2_ps,
         z2_ready, exp_in, exp_out, gate_ready, relu_ready, fused_ready, f_ps, x1_ready, pool_chain,
         setup_ready, split_ready, state_ready, var_a, rstd_a, dgs_ready, dgr_ready, rstd_first, var_first, tiny_ready, whi_ready) = (sem(n) for n in (
            "ln_nodes_ready", "ln_nodes_stored", "XA_loaded", "A1_ready", "Apk_ready", "Dg_ready", "adjT25_ps", "dbc_ps",
            "gwT_ps", "bp_ps", "R_ready", "dbc_sb", "gwT_sb", "bd_ready", "z_ps", "z_ready", "h_ps", "h_act", "h_dve",
            "s_ps", "s_ready", "sp_ps", "sp_ready", "z2_ps", "z2_ready", "exp_in", "exp_out", "gate_ready", "relu_ready",
            "fused_ready", "f_ps", "x1_ready", "pool_chain", "setup_ready", "split_ready",
            "state_ready", "var_a", "rstd_a", "dgs_ready", "dgr_ready", "rstd_first", "var_first", "tiny_ready", "whi_ready"))
        (io_ps, g_ps, gates_ready, cell_ready, tanh_ready, h1_ready, h32_ready, h2_ready, hc_ready,
         xn_ready, xT_ps, xbuf_ready, hT_ps, x2_ready, x2_stored, y_stats, y_aggr, y_rstd, y_ready, y_stored,
         deg_ready, degs_ready, dinv_ready, diag_ready, a_scaled, aT_ps, adjT_ready, x_stats, x_aggr, x_rstd, y_vareps, x_vareps) = (
            sem(n) for n in (
            "io_ps", "g_ps", "gates_ready", "cell_ready", "tanh_ready", "h1_ready", "h32_ready", "h2_ready", "hc_ready",
            "xn_ready", "xT_ps", "xbuf_ready", "hT_ps", "x2_ready", "x2_stored", "y_stats", "y_aggr", "y_rstd",
            "y_ready", "y_stored", "deg_ready", "degs_ready", "dinv_ready", "diag_ready", "a_scaled", "aT_ps",
            "adjT_ready", "x_stats", "x_aggr", "x_rstd", "y_vareps", "x_vareps"))
        adj_loaded = [sem(f"adj_loaded{i}") for i in range(2)]
        (ht_ps, hts_ready, c_ps, x3_ready, m_stats, m_aggr, m_vareps, m_rstd, xh_ready, xhT_ps, xnT_ready, xhi_ready,
         xlo_ready, logits_ps, router_chain, dif_ready, th_ready, wp_ready, wT_ps, wT_ready, l1_ps, wbc_ps, gelu_ready,
         gw_ready, ghi_ready, glo_ready, l2_ps, yT_ready, yo_ps, out_ready, cd_const, x3_copied) = (sem(n) for n in (
            "ht_ps", "hts_ready", "c_ps", "x3_ready", "m_stats", "m_aggr", "m_vareps", "m_rstd", "xh_ready", "xhT_ps",
            "xnT_ready", "xhi_ready", "xlo_ready", "logits_ps", "router_chain", "dif_ready", "th_ready", "wp_ready",
            "wT_ps", "wT_ready", "l1_ps", "wbc_ps", "gelu_ready", "gw_ready", "ghi_ready", "glo_ready", "l2_ps",
            "yT_ready", "yo_ps", "out_ready", "cd_const", "x3_copied"))
        cd_loaded = [sem(f"cd_loaded{i}") for i in range(2)]
        out_stored = [sem(f"out_stored{i}") for i in range(2)]

        tok = lambda a: a.rearrange("b (i s) d -> s b i d", s=TT)
        x_tok = tok(x_in)
        x2_v = x2_d.rearrange("(n p) d -> p n d", p=P)
        y_v = y_d.rearrange("(n p) d -> p n d", p=P)
        adj_v = adj_in.rearrange("b (c n) m -> n b c m", c=2)
        g_bank, io_bank = [PB[0], PB[1]], [PB[2], PB[3]]
        io_v = [p[:].rearrange("p (q n) -> p q n", q=2) for p in io_bank]

        def bc(ap, shape):
            return ap.to_broadcast(shape)

        def scan_flat(t):
            return t.rearrange("p b k -> p (b k)")

        nodes = lambda a: a[STEPS * B:, :].rearrange("(c m b) d -> m c (b d)", c=2, b=B)
        y_nodes, x2_nodes = nodes(y_d), nodes(x2_d)
        out_v = out.rearrange("b (c n) d -> n b c d", c=2)

        def iterations(eng, body):
            body(0, 0, 0)
            with eng.Fori(0, NB2 // 2 - 1) as it:
                body(it * 2 + 1, 1, it)
                body(it * 2 + 2, 0, it + 1)
            body(NB2 - 1, 1, NB2 // 2 - 1)

        block = ctx.enter_context(nc.Block())

        @block.sync
        def _(sp):
            for s in range(TT):
                sp.dma_start(X[s * B:(s + 1) * B, XPAD:XPAD + NTILE, :], x_tok[s, :, 0:NTILE, :]).then_inc(ld_x, 16)
            sp.dma_start(adj25[:], adj_in[:, 0:NN, 0:NN].rearrange("b n m -> n b m")).then_inc(ld_adj25, 16)
            sp.dma_start(const[:], io["consts"]).then_inc(ld_const, 16)
            sp.wait_ge(ln_nodes_ready, 1)
            sp.dma_start(ln_nodes_d.rearrange("(n p) d -> p n d", p=P), lnx[:]).then_inc(ln_nodes_stored, 16)
            sp.wait_ge(ln_nodes_stored, 16)
            sp.dma_start(XA, ln_nodes_d[0:NN * B, :].rearrange("(t b) d -> t b d", b=B)).then_inc(XA_loaded, 16)
            sp.dma_start(aW1[:], io["L0_gnn_W1"].rearrange("g d h -> d g h")).then_inc(ld_wa, 16)
            sp.dma_start(aW2[:], io["L0_gnn_W2"].rearrange("g (c h) d -> h g c d", c=2)).then_inc(ld_wa, 16)
            for s in range(TT):
                sp.dma_start(X[s * B:(s + 1) * B, XPAD + NTILE:XPAD + T // TT, :], x_tok[s, :, NTILE:, :]).then_inc(ld_x, 16)
            for i in range(2):
                sp.dma_start(adjn[i][:], adj_v[:, i]).then_inc(adj_loaded[i], 16)

            def group(G, k, more):
                sp.wait_ge(x2_ready, G + 1)
                sp.dma_start(x2_v[:, bass.ds(G * 2, 2), :], x2s[:]).then_inc(x2_stored, 16)
                sp.wait_ge(y_ready, G + 1)
                sp.dma_start(y_v[:, bass.ds(G * 2, 2), :], ys[:]).then_inc(y_stored, 16)
                if more:
                    sp.wait_ge(a_scaled, G + 1)
                    sp.dma_start(adjn[k][:], adj_v[:, bass.ds(G + 2, 1)].rearrange("n o c m -> n (o c) m")).then_inc(adj_loaded[k], 16)

            with sp.Fori(0, NGRP // 2 - 1) as it:
                for k in range(2):
                    group(it * 2 + k, k, True)
            for k in range(2):
                group(NGRP - 2 + k, k, False)
            group(NGRP, 0, False)
            sp.wait_ge(x2_stored, 16 * (NGRP + 1) + 1)
            sp.wait_ge(y_stored, 16 * (NGRP + 1) + 1)

            def load(f, par):
                sp.dma_start(yr[par][:], y_nodes[:, :, bass.ds(f * (2 * D), 2 * D)]).then_inc(cd_loaded[par], 16)
                sp.dma_start(x2r[par][:], x2_nodes[:, :, bass.ds(f * (2 * D), 2 * D)]).then_inc(cd_loaded[par], 16)

            def store(o, par):
                sp.wait_ge(out_ready, o + 1)
                sp.dma_start(out_v[:, bass.ds(o * 2, 2)], outb[par][:]).then_inc(out_stored[par], 16)

            def iteration(j, par, h):
                if not (isinstance(j, int) and j == NB2 - 1):
                    if not isinstance(j, int) or j + 2 < NB2:
                        sp.wait_ge(ht_ps, j + 1)
                        sp.wait_ge(x3_ready, j + 1)
                        load(j + 2, par)
                if not isinstance(j, int) or j > 0:
                    store(j - 1, 1 - par)

            sp.wait_ge(adjT_ready, 2 * NGRP)
            for f in range(2):
                load(f, f)
            iteration(0, 0, 0)
            with sp.Fori(0, NB2 // 2 - 2) as it:
                iteration(it * 2 + 1, 1, it)
                iteration(it * 2 + 2, 0, it + 1)
            iteration(NB2 - 3, 1, 0)
            iteration(NB2 - 2, 0, 0)
            iteration(NB2 - 1, 1, 0)
            store(NB2 - 1, 1)
            for par in range(2):
                sp.wait_ge(out_stored[par], 16 * NB2 // 2 + 1)

        @block.gpsimd
        def _(pool):
            count = [0]

            def link(ins):
                count[0] += 1
                ins.then_inc(pool_chain, 1)
                pool.wait_ge(pool_chain, count[0])

            tp = nc.gpsimd
            tp.memset(eps2[:], LN_EPS).then_inc(tiny_ready, 1)
            tp.memset(mhalf[:], -0.5).then_inc(tiny_ready, 1)
            tp.memset(tick[:], 0.0).then_inc(tiny_ready, 1)
            experts = [(wst[:].rearrange("p (e h) -> p e h", e=E), io["L1_ffn_W1"].rearrange("e d h -> d e h"))]
            experts += [(w2st[:, :, c, :], io["L1_ffn_W2"][:, c * P:(c + 1) * P, :].rearrange("e h d -> h e d")) for c in range(2)]
            experts += [(b2st[r * E:(r + 1) * E, :], io["L1_ffn_b2"]) for r in range(3)]
            for dst, src in experts:
                pool.dma_start(dst, src).then_inc(ld_wb, 16)
            pool.wait_ge(tiny_ready, 3)
            pool.wait_ge(var_a, 1)
            link(tp.tensor_tensor(rs_a[:], mv_a[:, :, 1], bc(eps2[:, 0:1], [P, NTILE]), ALU.add))
            tp.tensor_tensor(rs_a[:], rs_a[:], bc(mhalf[:, 0:1], [P, NTILE]), ALU.pow).then_inc(rstd_a, 1)
            tp.memset(S[:], 0.0).then_inc(gates_ready, 1)
            tp.memset(GC[:], 0.0).then_inc(hc_ready, 1)
            tp.memset(hs[1][:], 0.0).then_inc(state_ready, 1)
            tp.memset(h1[:], 0.0).then_inc(h1_ready, 1)
            tp.memset(h2[:], 0.0).then_inc(h2_ready, 1)
            tp.memset(x2s[:, 0, 0:1], 0.0).then_inc(x2_stored, 1)
            tp.memset(ys[:, 0, 0:1], 0.0).then_inc(y_stored, 1)
            tp.memset(X[:, 0:XPAD, :], 0.0).then_inc(state_ready, 1)
            tp.memset(X[:, XPAD + T // TT:, :], 0.0).then_inc(state_ready, 1)

            pool.wait_ge(A1_ready, 1)
            for i, (g, j, n, k) in enumerate(RUNS):
                tp.tensor_copy(Apk[:, :, OFF[g] + j:OFF[g] + j + k], A1[:, :, n:n + k]).then_inc(Apk_ready, 1)

            pool.wait_ge(ld_lstm, 16 * 10)
            link(tp.tensor_copy(vp[0][:], V[:]))
            link(tp.tensor_tensor(Vr[:], V[:], vp[0][:], ALU.subtract))
            link(tp.tensor_copy(vp[1][:], Vr[:]))
            link(tp.tensor_tensor(Vr[:], Vr[:], vp[1][:], ALU.subtract))
            link(tp.tensor_copy(vp[2][:], Vr[:]))
            link(tp.tensor_scalar(us[:], U[:], SC, None, ALU.mult))
            link(tp.tensor_scalar(bst[:, 0:3, :], bst[:, 0:3, :], SC, None, ALU.mult))
            link(tp.tensor_copy(bpa[0][:], bst[:]))
            link(tp.tensor_tensor(bra[:], bst[:], bpa[0][:], ALU.subtract))
            link(tp.tensor_copy(bpa[1][:], bra[:]))
            link(tp.tensor_tensor(bra[:], bra[:], bpa[1][:], ALU.subtract))
            link(tp.tensor_copy(bpa[2][:], bra[:]))
            pool.wait_ge(ld_const, 16)
            link(tp.tensor_scalar(bst[:], bpa[0][:], ident[0:3, 0:1], None, ALU.mult))
            for p in (1, 2):
                link(tp.tensor_scalar(bra[:], bpa[p][:], ident[0:3, p:p + 1], None, ALU.mult))
                link(tp.tensor_tensor(bst[:], bst[:], bra[:], ALU.add))
            link(tp.tensor_copy(brow[:], bst[:]))
            link(tp.tensor_copy(ones3[:, 0:P], ones[0:3, :]))
            link(tp.tensor_copy(ones3[:, P:2 * P], ones[0:3, :]))
            tp.tensor_copy(identb[:], ident).then_inc(setup_ready, 1)

            pool.wait_ge(ld_wb, 16 * len(experts))
            link(tp.tensor_copy(b2p[:, 0, :], b2st[:]))
            link(tp.tensor_tensor(b2ra[:], b2st[:], b2p[:, 0, :], ALU.subtract))
            link(tp.tensor_copy(b2p[:, 1, :], b2ra[:]))
            link(tp.tensor_tensor(b2rb[:], b2ra[:], b2p[:, 1, :], ALU.subtract))
            link(tp.tensor_copy(b2p[:, 2, :], b2rb[:]))
            tp.tensor_copy(sel_e[:], const[0:3 * E, C_SELE:C_SELE + E * P].rearrange("k (e p) -> k e p", e=E)).then_inc(split_ready, 1)

            pw = nc.gpsimd.tensor_tensor
            for G in range(2):
                pool.wait_ge(var_first, G + 1)
                link(pw(ve_x[:], mv_x[:, :, 1], eps2[:], ALU.add))
                pw(rs_x[:], ve_x[:], mhalf[:], ALU.pow).then_inc((rstd_first, x_rstd)[G], 1)

            def y_power(G):
                pool.wait_ge(y_aggr, G + 1)
                pw(ve_y[:], mv_y[:, :, 1], eps2[:], ALU.add).then_inc(y_vareps, 1)
                pool.wait_ge(y_vareps, G + 1)
                pw(rs_y[:], ve_y[:], mhalf[:], ALU.pow).then_inc(y_rstd, 1)

            with pool.Fori(0, NGRP // 2) as it:
                for k in range(2):
                    G = it * 2 + k
                    pool.wait_ge(degs_ready, G + 1)
                    pw(dinv[:], degs[:], mhalf[:], ALU.pow)
                    pw(sdiag[:], degs[:], bc(alpha[:, 0:1], [P, 2]), ALU.mult).then_inc(dinv_ready, 1)
                    y_power(G)
                    pool.wait_ge(x_aggr, G + 1)
                    pw(ve_x[:], mv_x[:, :, 1], eps2[:], ALU.add).then_inc(x_vareps, 1)
                    pool.wait_ge(x_vareps, G + 1)
                    pw(rs_x[:], ve_x[:], mhalf[:], ALU.pow).then_inc(x_rstd, 1)
            y_power(NGRP)

            pool.wait_ge(cd_loaded[0], 32)
            tp.memset(eps4[:], LN_EPS).then_inc(cd_const, 1)
            tp.memset(half4[:], -0.5).then_inc(cd_const, 1)
            for i in range(2):
                tp.memset(outb[i][:, 0, 0, 0:1], 0.0).then_inc(out_stored[i], 1)
            pool.wait_ge(cd_const, 2)

            def m_power(f):
                pool.wait_ge(m_aggr, f + 1)
                pw(ve_m[:], mv_m[:, :, 1], eps4[:], ALU.add).then_inc(m_vareps, 1)
                pool.wait_ge(m_vareps, f + 1)
                pw(rs_m[:], ve_m[:], half4[:], ALU.pow).then_inc(m_rstd, 1)

            def keep_x3(f, par, fh):
                pool.wait_ge(out_stored[par], fh * 16 + 1)
                pw(outb[par][:], x3[par][:], bc(ones[:, 0:1].unsqueeze(2).unsqueeze(3), [P, 2, 2, D]), ALU.mult).then_inc(x3_copied, 1)

            for f in range(2):
                m_power(f)
                keep_x3(f, f, 0)
            with pool.Fori(0, NB2 // 2 - 1) as it:
                for par in range(2):
                    m_power(it * 2 + (2 + par))
                    keep_x3(it * 2 + (2 + par), par, it + 1)

        @block.tensor
        def _(pe):
            mm = nc.tensor.matmul
            tr = nc.tensor.transpose
            pe.wait_ge(ld_const, 16)
            pe.wait_ge(A1_ready, 1)
            for c in range(2):
                for b in range(16):
                    m = tr(PB[c][0:NN, b * NN:(b + 1) * NN], A1[:, c * 16 + b, :], ident[0:NN, 0:NN])
                m.then_inc(adjT25_ps, 1)
            pe.wait_ge(Dg_ready, 1)
            for c in range(4):
                mm(PB[2 + c][:, 0:8 * NP], ones[0:NN, :], scan_flat(Dg[:, 8 * c:8 * c + 8, :]), start=True, stop=True).then_inc(dbc_ps, 1)
            pe.wait_ge(ld_small, 16 * 10)
            tr(PB[6][:, 0:P], gw[:], ident)
            tr(PB[6][:, P:P + NV], vrows[:], ident[0:NV, 0:NV]).then_inc(gwT_ps, 1)
            pe.wait_ge(Apk_ready, len(RUNS))
            for c in range(2):
                if c == 1:
                    pe.wait_ge(gwT_sb, 1)
                for i in range(8):
                    q = 8 * c + i
                    m = mm(PB[7 - c][0:2 * NP, i * NP:(i + 1) * NP], scan_flat(Apk[:, 2 * q:2 * q + 2, :]), const[0:NN, C_SEL:C_SEL + NP], start=(i == 0), stop=True, skip_group_check=True)
                m.then_inc(bp_ps, 1)
            pe.wait_ge(XA_loaded, 16)
            for c in range(4):
                pe.wait_ge(R_ready, 2)
                if c >= 2:
                    pe.wait_ge(dbc_sb, c - 1)
                for i in range(8):
                    b = 8 * c + i
                    m = mm(PB[c][:, i * NP:(i + 1) * NP], XA[:, b, :], R[:, b, :], start=(i == 0), stop=True, skip_group_check=True)
                m.then_inc(z_ps, 1)
            pe.wait_ge(ld_wa, 32)
            pe.wait_ge(z_ready, 4)
            pe.wait_ge(dbc_sb, 4)
            hb = [PB[4], PB[5], PB[0], PB[1]]
            for i in range(2 * len(HCHUNKS)):
                g, b0, b1 = HCHUNKS[i // 2]
                if i >= 4:
                    pe.wait_ge((h_act, h_dve)[i % 2], (i - 4) // 2 + 1)
                n = len(GROUPS[g])
                mm(hb[i % 4][:, 0:(b1 - b0) * n], aW1[:, g, (i % 2) * P:(i % 2 + 1) * P], Z[:, b0:b1, OFF[g]:OFF[g + 1]], start=True, stop=True).then_inc(h_ps, 1)
            for i, (g, b0, b1) in enumerate(HCHUNKS):
                pe.wait_ge(h_act, i + 1)
                pe.wait_ge(h_dve, i + 1)
                if i >= 2:
                    pe.wait_ge(s_ready, i - 1)
                n = len(GROUPS[g])
                for c in range(2):
                    m = mm(PB[2 + i % 2][:, 0:(b1 - b0) * n], aW2[:, g, c, :], Hh[:, c, b0:b1, OFF[g]:OFF[g + 1]], start=(c == 0), stop=(c == 1))
                m.then_inc(s_ps, 1)
            pe.wait_ge(s_ready, len(HCHUNKS))
            for c in range(4):
                for i in range(4):
                    q = 4 * c + i
                    m = tr(hb[c][0:2 * NP, i * P:(i + 1) * P], scan_flat(St[:, 2 * q:2 * q + 2, :]), ident)
                m.then_inc(sp_ps, 1)
            pe.wait_ge(bd_ready, 2)
            for c in range(4):
                pe.wait_ge(sp_ready, c + 1)
                bank = (PB[2], PB[3], PB[6], PB[7])[c]
                for i in range(4):
                    q = 4 * c + i
                    m = mm(bank[:, i * 2 * NP:(i + 1) * 2 * NP], Sp[:, q, :], scan_flat(Bd[:, q, :, :]), start=(i == 0), stop=True, skip_group_check=True)
                m.then_inc(z2_ps, 1)
            pe.wait_ge(fused_ready, 1)
            for i in range(NTILE):
                m = tr(PB[4 + i // 4][:, (i % 4) * P:(i % 4 + 1) * P], fused[:, i * TT:(i + 1) * TT, :].rearrange("p t b -> p (t b)"), ident)
                if i in (3, NTILE - 1):
                    m.then_inc(f_ps, 1)

            def x_transpose():
                for i in range(2):
                    m = tr(PB[4][:, i * P:(i + 1) * P], xn[:, i, :], ident)
                m.then_inc(xT_ps, 1)

            def x_gate(k, q):
                o = g_bank[k][:, 0:STEPS * B] if q == 2 else io_v[k][:, q, :]
                mm(o, us[:, q, :], xbuf[:], start=(q != 1), stop=False, skip_group_check=True)

            def biases(k):
                for q in range(3):
                    o = g_bank[k][:, 0:STEPS * B] if q == 2 else io_v[k][:, q, :]
                    mm(o, brow[:, q, :], ones3[:], start=False, stop=False, skip_group_check=True)

            pe.wait_ge(x1_ready, 2)
            pe.wait_ge(xn_ready, 1)
            x_transpose()
            pe.wait_ge(setup_ready, 1)
            pe.wait_ge(xbuf_ready, 1)
            for q in (0, 1, 2):
                x_gate(0, q)
            biases(0)
            pe.wait_ge(state_ready, 3)

            with pe.Fori(0, NGRP // 4) as it:
                for q4 in range(4):
                    G, k = it * 4 + q4, q4 % 2
                    for s in range(STEPS):
                        t = it * (4 * STEPS) + (q4 * STEPS + s)
                        cols = slice(s * B, (s + 1) * B)

                        def gate(q, p, h):
                            o = g_bank[k][:, cols] if q == 2 else io_v[k][:, q, cols]
                            return mm(o, vp[p][:, q, :], h[:], start=False, stop=True, skip_group_check=True)

                        pe.wait_ge(h1_ready, t + 1)
                        for q in (0, 1, 2):
                            for p in range(3):
                                gate(q, p, h1)
                        pe.wait_ge(h2_ready, t + 1)
                        for q in (0, 1):
                            for p in range(2):
                                m = gate(q, p, h2)
                        m.then_inc(io_ps, 1)
                        for p in range(2):
                            m = gate(2, p, h2)
                        m.then_inc(g_ps, 1)
                        if s == 0:
                            for i in range(2):
                                m = tr(PB[5][:, i * P:(i + 1) * P], hs[1 - k][:, i * P:(i + 1) * P], ident)
                            m.then_inc(hT_ps, 1)
                        if s == 1:
                            pe.wait_ge(xn_ready, G + 2)
                            x_transpose()
                        if s in (3, 4, 5):
                            if s == 3:
                                pe.wait_ge(xbuf_ready, G + 2)
                            x_gate(1 - k, s - 3)
                        if s == 7:
                            biases(1 - k)
                        if s == 6:
                            pe.wait_ge(a_scaled, G + 1)
                            for c in range(2):
                                for n in range(2):
                                    m = tr(PB[6][:, c * T + n * P:c * T + (n + 1) * P], adjs[:, n, c * P:(c + 1) * P], ident)
                            m.then_inc(aT_ps, 1)
            pe.wait_ge(h2_ready, T + 1)
            for i in range(2):
                m = tr(PB[5][:, i * P:(i + 1) * P], hs[1][:, i * P:(i + 1) * P], ident)
            m.then_inc(hT_ps, 1)

            H = [[PB[0], PB[1]], [PB[2], PB[3]]]
            yT_b, wbc_b, fa, fb = PB[4], PB[5], PB[6], PB[7]

            def aggregate(f, par, fh):
                pe.wait_ge(cd_loaded[par], fh * 32 + 32)
                for bb in range(2):
                    for c in range(2):
                        m = mm(fa[:, bb * T:(bb + 1) * T], yr[par][:, c, bb * D:(bb + 1) * D],
                               adjT[:, bass.ds(f * 2 + bb, 1), c, :].rearrange("p o n -> p (o n)"),
                               start=(bb == 0 and c == 0), stop=(c == 1), skip_group_check=True)
                m.then_inc(ht_ps, 1)

            def project(f):
                for i in range(4):
                    mm(fb[:, i * P:(i + 1) * P], ones3[:, 0:P], brow[:, 3, :], start=(i == 0), stop=False, skip_group_check=True)
                pe.wait_ge(hts_ready, f + 1)
                for i in range(4):
                    m = mm(fb[:, i * P:(i + 1) * P], hts[:, i * P:(i + 1) * P], gnn_wT[:], start=False, stop=True, skip_group_check=True)
                m.then_inc(c_ps, 1)

            def normed_transpose(f):
                pe.wait_ge(xh_ready, f + 1)
                for i in range(4):
                    m = tr(fa[:, i * P:(i + 1) * P], xh[:, i, :], ident)
                m.then_inc(xhT_ps, 1)

            def logits(f):
                pe.wait_ge(xnT_ready, f + 1)
                for i in range(4):
                    m = mm(fb[:, i * E:(i + 1) * E], xnT[:, i * P:(i + 1) * P], wr[:], start=(i == 0), stop=True, skip_group_check=True)
                m.then_inc(logits_ps, 1)

            def weights_transpose(f):
                pe.wait_ge(wp_ready, f + 1)
                for i in range(4):
                    m = mm(fb[0:3 * E, i * P:(i + 1) * P], wp[:, i, :, :].rearrange("p k e -> p (k e)"), identb[:], start=(i == 0), stop=True, skip_group_check=True)
                m.then_inc(wT_ps, 1)

            def layer1(n, e, par):
                if n is not None:
                    pe.wait_ge(gelu_ready, n)
                for c in range(2):
                    for k, (w, x) in enumerate(((w1hi, xhi), (w1lo, xhi), (w1hi, xlo))):
                        m = mm(H[e % 2][c][:], w[:, e, c * P:(c + 1) * P], x[par][:], start=(k == 0), stop=(k == 2))
                m.then_inc(l1_ps, 1)

            def weight_rows(n, e, par):
                if n is not None:
                    pe.wait_ge(gw_ready, n)
                mm(wbc_b[:], sel_e[:, e, :], wT[par][:], start=True, stop=True).then_inc(wbc_ps, 1)

            def layer2(n, e, par):
                if e == 0:
                    for i in range(3):
                        mm(yT_b[:], b2p[:, i, :], wT[par][:], start=(i == 0), stop=False, skip_group_check=True)
                pe.wait_ge(glo_ready, n + 1)
                k = 0
                for c in range(2):
                    for w, g in ((w2hi, ghi), (w2lo, ghi), (w2hi, glo)):
                        k += 1
                        m = mm(yT_b[:], w[:, e, c, :], g[e % 4][:, c, :], start=False, stop=(e == E - 1 and k == 6), skip_group_check=True)
                m.then_inc(l2_ps, 1)

            def out_transpose(o):
                pe.wait_ge(yT_ready, o + 1)
                for i in range(4):
                    m = tr(fb[:, i * P:(i + 1) * P], yTs[:, i * P:(i + 1) * P], ident)
                m.then_inc(yo_ps, 1)

            pe.wait_ge(adjT_ready, 2 * NGRP)
            pe.wait_ge(x2_ready, NGRP + 1)
            aggregate(0, 0, 0)
            project(0)
            normed_transpose(0)
            logits(0)
            weights_transpose(0)
            pe.wait_ge(xlo_ready, 1)
            pe.wait_ge(wT_ready, 1)

            def iteration(j, par, h):
                first, last = (isinstance(j, int) and j == q for q in (0, NB2 - 1))
                f, fpar = j + 1, 1 - par
                for e in range(E):
                    n = j * E + e
                    if e == 0:
                        if not last:
                            aggregate(f, fpar, h + par)
                        pe.wait_ge(xlo_ready, j + 1)
                    layer1(None if first and e < 2 else n - 1, e, par)
                    if not (first and e < LAG):
                        if e == LAG and not first:
                            pe.wait_ge(yT_ready, j)
                        layer2(n - LAG, (e - LAG) % E, par if e >= LAG else 1 - par)
                    if e == 0:
                        pe.wait_ge(wT_ready, j + 1)
                    weight_rows(None if first and e < 1 else n, e, par)
                    if not last:
                        if e == 0:
                            project(f)
                        if e == 3:
                            normed_transpose(f)
                        if e == 4:
                            if not first:
                                pe.wait_ge(out_ready, j)
                            logits(f)
                        if e == 7:
                            weights_transpose(f)
                    if e == 3 and not first:
                        out_transpose(j - 1)

            iterations(pe, iteration)
            n = NB2 * E
            for i in range(LAG, 0, -1):
                layer2(n - i, E - i, 1)
            pe.wait_ge(out_ready, NB2 - 1)
            out_transpose(NB2 - 1)

        @block.scalar
        def _(act):
            av = nc.scalar.activation
            bsrc = ("L0_ffn_b_i", "L0_ffn_b_o", "L0_ffn_b_c", "L1_gnn_b")
            small = [(V[:, q, :], io[n]) for q, n in enumerate(("L0_ffn_V_i", "L0_ffn_V_o", "L0_ffn_V_c"))]
            small += [(U[:, q, :], io[n]) for q, n in enumerate(("L0_ffn_U_i", "L0_ffn_U_o", "L0_ffn_U_c"))]
            small += [(bst[:, q, :], io[n].partition_broadcast(3)) for q, n in enumerate(bsrc)]
            for dst, src in small:
                act.dma_start(dst, src).then_inc(ld_lstm, 16)
            more = [(fw[:], io["L0_gnn_fusion_w"].partition_broadcast(P)),
                    (vrows[0:2 * NG, :], io["L0_gnn_b1"].rearrange("g (c h) -> (g c) h", c=2)),
                    (vrows[2 * NG:3 * NG, :], io["L0_gnn_b2"]),
                    (vrows[3 * NG:3 * NG + 1, :], io["L1_ffn_gamma"].unsqueeze(0)),
                    (vrows[3 * NG + 1:3 * NG + 2, :], io["L1_ffn_beta"].unsqueeze(0)),
                    (vrows[3 * NG + 2:, :], io["L1_ffn_b1"].rearrange("e (c h) -> (e c) h", c=2)),
                    (gw[:], io["L1_gnn_W"]),
                    (alpha[:], io["L1_gnn_alpha"].partition_broadcast(P)),
                    (wr[:], io["L1_ffn_Wr"]),
                    (br[:], io["L1_ffn_br"].partition_broadcast(P))]
            for dst, src in more:
                act.dma_start(dst, src).then_inc(ld_small, 16)
            act.wait_ge(dgs_ready, 1)
            av(dgr[:], dgs[:], ACT.Sqrt).then_inc(dgr_ready, 1)
            act.wait_ge(exp_in, 1)
            av(fe[:], fw[:], ACT.Exp, bias=fmax[:, 0:1], accum_out=fs[:]).then_inc(exp_out, 1)
            for c in range(4):
                act.wait_ge(dbc_ps, c + 1)
                av(scan_flat(Dbc[:, 8 * c:8 * c + 8, :]), PB[2 + c][:, 0:8 * NP], ACT.Copy).then_inc(dbc_sb, 1)
            act.wait_ge(gwT_ps, 1)
            av(gnn_wT[:], PB[6][:, 0:P], ACT.Copy)
            av(vcols[:], PB[6][:, P:P + NV], ACT.Copy).then_inc(gwT_sb, 1)
            act.wait_ge(gwT_sb, 1)
            act.wait_ge(ld_wb, 16 * 6)
            av(w1hi[:], wst[:].rearrange("p (e h) -> p e h", e=E), ACT.Copy).then_inc(whi_ready, 1)
            av(w2hi[:], w2st[:], ACT.Copy).then_inc(whi_ready, 1)
            hb = [PB[4], PB[5], PB[0], PB[1]]
            for i in range(0, 2 * len(HCHUNKS), 2):
                g, b0, b1 = HCHUNKS[i // 2]
                n = len(GROUPS[g])
                act.wait_ge(h_ps, i + 1)
                av(Hh[:, 0, b0:b1, OFF[g]:OFF[g + 1]], hb[i % 4][:, 0:(b1 - b0) * n].rearrange("p (b n) -> p b n", n=n),
                   ACT.Relu, bias=ab1[:, g, 0:1]).then_inc(h_act, 1)
            for c in range(4):
                act.wait_ge(sp_ps, c + 1)
                av(Sp[:, 4 * c:4 * c + 4, :].rearrange("p q d -> p (q d)"), hb[c][0:2 * NP, :], ACT.Copy).then_inc(sp_ready, 1)
            act.wait_ge(z2_ready, 4)
            act.wait_ge(gate_ready, 1)
            for g in range(NG):
                n = len(GROUPS[g])
                dst = fused[:, 0:NN, :].rearrange("p t b -> p b t") if g == 0 else O[:, :, OFF[g]:OFF[g + 1]]
                av(dst, Z2[:, :, OFF[g]:OFF[g + 1]], ACT.Relu, scale=gwt[:, g:g + 1], bias=gb2[:, g:g + 1]).then_inc(relu_ready, 1)

            def x_evacuate():
                return av(xbuf[:], PB[4][:, 0:STEPS * B], ACT.Copy)

            act.wait_ge(xT_ps, 1)
            x_evacuate().then_inc(xbuf_ready, 1)
            act.wait_ge(state_ready, 3)
            act.wait_ge(split_ready, 1)
            with act.Fori(0, NGRP // 4) as it:
                for q4 in range(4):
                    G, k = it * 4 + q4, q4 % 2
                    for s in range(STEPS):
                        t = it * (4 * STEPS) + (q4 * STEPS + s)
                        cols = slice(s * B, (s + 1) * B)
                        act.wait_ge(io_ps, t + 1)
                        av(S[:, :, :, 1], io_v[k][:, :, cols], ACT.Sigmoid, scale=1 / SC)
                        act.wait_ge(g_ps, t + 1)
                        av(GC[:, :, 0], g_bank[k][:, cols], ACT.Tanh, scale=1 / SC).then_inc(gates_ready, 1)
                        act.wait_ge(cell_ready, t + 1)
                        av(tanh_c[:], CC[:, :, 1], ACT.Tanh).then_inc(tanh_ready, 1)
                        if s == 0:
                            act.wait_ge(adj_loaded[k], it * 32 + (q4 // 2 * 16 + 16))
                            av(junk[:], adjn[k][:, 0, :], ACT.Copy, accum_out=deg[:, 0:1])
                        if s == 2:
                            act.wait_ge(xT_ps, G + 2)
                            x_evacuate().then_inc(xbuf_ready, 1)
                        if s == 1:
                            av(junk[:], adjn[k][:, 1, :], ACT.Copy, accum_out=deg[:, 1:2]).then_inc(deg_ready, 1)
                        if s in (6, 7):
                            c = s - 6
                            act.wait_ge(aT_ps, G + 1)
                            av(junk[:, 0:1], ident[:, 0:1], ACT.Copy)
                            av(adjT[:, bass.ds(G, 1), c, :].rearrange("p o n -> p (o n)"), PB[6][:, c * T:(c + 1) * T], ACT.Copy,
                               scale=dinv[:, c:c + 1]).then_inc(adjT_ready, 1)

            def aggregate_evacuate(f):
                act.wait_ge(ht_ps, f + 1)
                av(hts[:], PB[6][:], ACT.Copy).then_inc(hts_ready, 1)

            def scaled_evacuate(f, par):
                act.wait_ge(xhT_ps, f + 1)
                av(xnT[:], PB[6][:], ACT.Identity, scale=gamma, bias=beta).then_inc(xnT_ready, 1)
                av(xhi[par][:], PB[6][:], ACT.Identity, scale=gamma, bias=beta).then_inc(xhi_ready, 1)

            def router_tanh(f):
                act.wait_ge(dif_ready, f + 1)
                av(th[:], dif[:], ACT.Tanh, scale=0.5).then_inc(th_ready, 1)

            def weights_evacuate(f, par):
                act.wait_ge(wT_ps, f + 1)
                av(wT[par][:], PB[7][0:3 * E, :], ACT.Copy).then_inc(wT_ready, 1)

            def upper_half(n, e, ring=True):
                if ring:
                    act.wait_ge(l2_ps, n - 3)
                act.wait_ge(gw_ready, n + 1)
                av(ghi[e % 4][:], Gw[e % 2][:], ACT.Copy).then_inc(ghi_ready, 1)

            def y_evacuate(o):
                act.wait_ge(l2_ps, o * E + E)
                av(yTs[:], PB[4][:], ACT.Copy).then_inc(yT_ready, 1)

            aggregate_evacuate(0)
            scaled_evacuate(0, 0)
            router_tanh(0)
            weights_evacuate(0, 0)

            def iteration(j, par, h):
                first, last = (isinstance(j, int) and j == q for q in (0, NB2 - 1))
                f, fpar = j + 1, 1 - par
                for e in range(E):
                    n = j * E + e
                    if e == 0 and not last:
                        aggregate_evacuate(f)
                    act.wait_ge(l1_ps, n + 1)
                    for c in range(2):
                        a = av(Gl[e % 2][:, c, :], PB[2 * (e % 2) + c][:], ACT.Gelu, bias=eb1[:, e, c:c + 1])
                    a.then_inc(gelu_ready, 1)
                    if not (first and e < 1):
                        upper_half(n - 1, (e - 1) % E, not (first and e < 5))
                    if not last:
                        if e == 3:
                            scaled_evacuate(f, fpar)
                        if e == 5:
                            router_tanh(f)
                        if e == 7:
                            weights_evacuate(f, fpar)
                    if e == LAG - 1 and not first:
                        y_evacuate(j - 1)

            iterations(act, iteration)
            upper_half(NB2 * E - 1, E - 1)
            y_evacuate(NB2 - 1)

        @block.vector
        def _(dve):
            v = nc.vector
            count = [0]

            def link(ins):
                count[0] += 1
                ins.then_inc(chain, 1)
                dve.wait_ge(chain, count[0])

            dve.wait_ge(ld_x, 16 * TT)
            for i in range(NTILE):
                ins = v.bn_stats(st_a[:, i, :], X[:, XPAD + i, :])
            link(ins)
            for i in range(NTILE):
                ins = v.bn_aggr(mv_a[:, i, :], st_a[:, i, :])
            ins.then_inc(var_a, 1)
            dve.wait_ge(rstd_a, 1)
            for i in range(NTILE):
                ins = v.tensor_scalar(lnx[:, i, :], X[:, XPAD + i, :], mv_a[:, i, 0:1], rs_a[:, i:i + 1], ALU.subtract, ALU.mult)
            ins.then_inc(ln_nodes_ready, 1)
            dve.wait_ge(ld_adj25, 16)
            dve.wait_ge(ld_const, 16)
            ins = v.tensor_tensor(A1[:], adj25[:], bc(ident[0:NN, 0:NN].unsqueeze(1), [NN, B, NN]), ALU.add)
            ins.then_inc(A1_ready, 1)
            dve.wait_ge(A1_ready, 1)
            v.tensor_reduce(dg[:, 0, :], A1[:], AXX, ALU.add)
            v.tensor_reduce(dg[:, 1, :], A1[:, :, 0:9], AXX, ALU.add)
            link(v.tensor_reduce(seg[:], A1[:, :, 0:15].rearrange("n b (s k) -> n b s k", k=3), AXX, ALU.add))
            v.tensor_tensor(dg[:, 2, :], seg[:, :, 3], seg[:, :, 4], ALU.add)
            v.tensor_tensor(dg[:, 3, :], seg[:, :, 2], seg[:, :, 4], ALU.add)
            link(v.tensor_tensor(dg[:, 4, :], seg[:, :, 1], seg[:, :, 3], ALU.add))
            link(v.tensor_tensor(dg[:, 2, :], dg[:, 2, :], A1[:, :, 0], ALU.add))
            link(v.tensor_tensor(dgm[:], dg[:], bc(const[0:NN, C_M5:C_M5 + NG].unsqueeze(2), [NN, NG, B]), ALU.mult))
            v.scalar_tensor_tensor(out=dgs[:], in0=dgm[:], scalar=0.0, in1=dgm[:], op0=ALU.is_equal, op1=ALU.add).then_inc(dgs_ready, 1)
            dve.wait_ge(dgr_ready, 1)
            link(v.reciprocal(dgr[:], dgr[:]))
            link(v.scalar_tensor_tensor(out=dgi[:], in0=dgm[:], scalar=0.0, in1=dgr[:], op0=ALU.not_equal, op1=ALU.mult))
            for g in range(NG):
                n = len(GROUPS[g])
                ins = v.tensor_tensor(Dg[:, :, OFF[g]:OFF[g + 1]], bc(const[0:NN, C_SEL + OFF[g]:C_SEL + OFF[g + 1]].unsqueeze(1), [NN, B, n]),
                                      bc(dgi[:, g, :].unsqueeze(2), [NN, B, n]), ALU.mult)
            ins.then_inc(Dg_ready, 1)
            for c in range(2):
                dve.wait_ge(adjT25_ps, c + 1)
                src = PB[c][0:NN, 0:16 * NN].rearrange("p (b n) -> p b n", n=NN)
                for g, j, n, k in RUNS:
                    ins = v.tensor_tensor(R[:, 16 * c:16 * c + 16, OFF[g] + j:OFF[g] + j + k], src[:, :, n:n + k],
                                          bc(dgi[:, g, 16 * c:16 * c + 16].unsqueeze(2), [NN, 16, k]), ALU.mult)
                ins.then_inc(R_ready, 1)
            dve.wait_ge(ld_small, 16 * 10)
            link(v.tensor_reduce(fmax[:], fw[:], AXX, ALU.max))
            v.tensor_scalar(fmax[:], fmax[:], -1.0, None, ALU.mult).then_inc(exp_in, 1)
            for c in range(2):
                dve.wait_ge(bp_ps, c + 1)
                src = PB[7 - c][0:2 * NP, 0:8 * NP].rearrange("p (q n) -> p q n", n=NP)
                mask = const[0:2 * NP, C_MASK:C_MASK + 2 * NP].rearrange("p (b n) -> p b n", b=2)
                v.tensor_tensor(Bd[:, 8 * c:8 * c + 8, :, :], bc(src.unsqueeze(2), [2 * NP, 8, 2, NP]),
                                bc(mask.unsqueeze(1), [2 * NP, 8, 2, NP]), ALU.mult).then_inc(bd_ready, 1)
            for c in range(4):
                dve.wait_ge(dbc_sb, c + 1)
                dve.wait_ge(z_ps, c + 1)
                v.tensor_tensor(scan_flat(Z[:, 8 * c:8 * c + 8, :]), PB[c][:, 0:8 * NP], scan_flat(Dbc[:, 8 * c:8 * c + 8, :]), ALU.mult).then_inc(z_ready, 1)
            v.memset(fused[:, NN:, :], 0.0)
            dve.wait_ge(whi_ready, 1)
            v.tensor_tensor(w1lo[:], wst[:].rearrange("p (e h) -> p e h", e=E), w1hi[:].bitcast(F32), ALU.subtract)
            dve.wait_ge(gwT_sb, 1)
            hb = [PB[4], PB[5], PB[0], PB[1]]
            for i in range(1, 2 * len(HCHUNKS), 2):
                g, b0, b1 = HCHUNKS[i // 2]
                n = len(GROUPS[g])
                dve.wait_ge(h_ps, i + 1)
                v.tensor_scalar(Hh[:, 1, b0:b1, OFF[g]:OFF[g + 1]], hb[i % 4][:, 0:(b1 - b0) * n].rearrange("p (b n) -> p b n", n=n),
                                ab1[:, g, 1:2], 0.0, ALU.add, ALU.max).then_inc(h_dve, 1)
            for i, (g, b0, b1) in enumerate(HCHUNKS):
                n = len(GROUPS[g])
                dve.wait_ge(s_ps, i + 1)
                v.tensor_tensor(St[:, b0:b1, OFF[g]:OFF[g + 1]], PB[2 + i % 2][:, 0:(b1 - b0) * n].rearrange("p (b n) -> p b n", n=n),
                                Dbc[:, b0:b1, OFF[g]:OFF[g + 1]], ALU.mult).then_inc(s_ready, 1)
            dve.wait_ge(whi_ready, 2)
            v.tensor_tensor(w2lo[:], w2st[:], w2hi[:].bitcast(F32), ALU.subtract)
            dve.wait_ge(exp_out, 1)
            link(v.reciprocal(fr[:], fs[:]))
            link(v.tensor_scalar(gwt[:], fe[:], fr[:, 0:1], None, ALU.mult))
            v.tensor_tensor(gb2[:], gwt[:], ab2, ALU.mult).then_inc(gate_ready, 1)
            v.tensor_scalar(alpha[:], alpha[:], 1e-10, None, ALU.max)
            for c in range(4):
                dve.wait_ge(z2_ps, c + 1)
                bank = (PB[2], PB[3], PB[6], PB[7])[c]
                v.tensor_tensor(scan_flat(Z2[:, 8 * c:8 * c + 8, :]), bank[:, 0:8 * NP], scan_flat(Dbc[:, 8 * c:8 * c + 8, :]), ALU.mult).then_inc(z2_ready, 1)
            for g, j, n, k in RUNS:
                if g:
                    dve.wait_ge(relu_ready, g + 1)
                    f = fused[:, n:n + k, :]
                    link(v.tensor_tensor(f, f, O[:, :, OFF[g] + j:OFF[g] + j + k].rearrange("p b k -> p k b"), ALU.add))
            v.memset(deg[:], 0.0).then_inc(fused_ready, 1)
            for c in range(2):
                dve.wait_ge(f_ps, c + 1)
                n = min(4, NTILE - 4 * c)
                xs = X[:, XPAD + 4 * c:XPAD + 4 * c + n, :]
                v.tensor_tensor(xs, PB[4 + c][:, 0:n * P].rearrange("p (i d) -> p i d", d=D), xs, ALU.add).then_inc(x1_ready, 1)

            for G in range(2):
                dve.wait_ge(x1_ready, 1)
                for i in range(2):
                    ins = v.bn_stats(st_x[:, i, :], X[:, XPAD + 2 * G + i, :])
                link(ins)
                for i in range(2):
                    ins = v.bn_aggr(mv_x[:, i, :], st_x[:, i, :])
                ins.then_inc(var_first, 1)
                dve.wait_ge((rstd_first, x_rstd)[G], 1)
                if G == 0:
                    for i in range(2):
                        ins = v.tensor_scalar(xn[:, i, :], X[:, XPAD + i, :], mv_x[:, i, 0:1], rs_x[:, i:i + 1], ALU.subtract, ALU.mult)
                    ins.then_inc(xn_ready, 1)
                    dve.wait_ge(xn_ready, 1)
            dve.wait_ge(x1_ready, 2)
            dve.wait_ge(ld_x, 32 * TT)
            dve.wait_ge(state_ready, 3)
            dve.wait_ge(tiny_ready, 3)
            dve.wait_ge(xT_ps, 1)

            def y_norm(G):
                for i in range(2):
                    ins = v.tensor_scalar(ys[:, i, :], x2s[:, i, :], mv_y[:, i, 0:1], rs_y[:, i:i + 1], ALU.subtract, ALU.mult)
                ins.then_inc(y_ready, 1)

            def h_scaled_add(G, i):
                return v.scalar_tensor_tensor(out=x2s[:, i, :], in0=PB[5][:, i * P:(i + 1) * P], scalar=1 / SC,
                                              in1=X[:, bass.ds(G * 2 + i, 1), :].rearrange("p o d -> p (o d)"), op0=ALU.mult, op1=ALU.add)

            def fill(G, k, s, it):
                def x_tile(i):
                    return X[:, bass.ds(G * 2 + (4 + i), 1), :].rearrange("p o d -> p (o d)")

                if s == 0:
                    dve.wait_ge(x_rstd, G + 1)
                    for i in range(2):
                        ins = v.tensor_scalar(xn[:, i, :], x_tile(i), mv_x[:, i, 0:1], rs_x[:, i:i + 1], ALU.subtract, ALU.mult)
                    ins.then_inc(xn_ready, 1)
                if s == 1:
                    dve.wait_ge(hT_ps, G + 1)
                    dve.wait_ge(x2_stored, G * 16 + 1)
                    h_scaled_add(G, 0)
                    h_scaled_add(G, 1).then_inc(x2_ready, 1)
                if s == 2:
                    dve.wait_ge(deg_ready, G + 1)
                    v.scalar_tensor_tensor(out=degs[:], in0=deg[:], scalar=0.0, in1=deg[:], op0=ALU.is_equal, op1=ALU.add).then_inc(degs_ready, 1)
                    dve.wait_ge(x2_ready, G + 1)
                    for i in range(2):
                        ins = v.bn_stats(st_y[:, i, :], x2s[:, i, :])
                    ins.then_inc(y_stats, 1)
                if s in (3, 4):
                    c = s - 3
                    if s == 3:
                        dve.wait_ge(y_stats, G + 1)
                        dve.wait_ge(dinv_ready, G + 1)
                    a = adjn[k][:, c, c * P:(c + 1) * P]
                    ins = v.scalar_tensor_tensor(out=a, in0=ident, scalar=sdiag[:, c:c + 1], in1=a, op0=ALU.mult, op1=ALU.add)
                    if s == 4:
                        ins.then_inc(diag_ready, 1)
                if s == 3:
                    for i in range(2):
                        ins = v.bn_aggr(mv_y[:, i, :], st_y[:, i, :])
                    ins.then_inc(y_aggr, 1)
                if s == 4:
                    dve.wait_ge(y_stored, G * 16 + 1)
                    dve.wait_ge(y_rstd, G + 1)
                    y_norm(G)
                if s == 5:
                    dve.wait_ge(diag_ready, G + 1)
                    for c in range(2):
                        ins = v.tensor_scalar(adjs[:, c, :], adjn[k][:, c, :], dinv[:, c:c + 1], None, ALU.mult)
                    ins.then_inc(a_scaled, 1)
                if s == 6:
                    for i in range(2):
                        ins = v.bn_stats(st_x[:, i, :], x_tile(i + 2))
                    ins.then_inc(x_stats, 1)
                if s == 7:
                    dve.wait_ge(x_stats, G + 1)
                    v.memset(tick[:, 0:1], 0.0)
                    for i in range(2):
                        ins = v.bn_aggr(mv_x[:, i, :], st_x[:, i, :])
                    ins.then_inc(x_aggr, 1)

            with dve.Fori(0, NGRP // 4) as it:
                for q4 in range(4):
                    G, k = it * 4 + q4, q4 % 2
                    for s in range(STEPS):
                        t = it * (4 * STEPS) + (q4 * STEPS + s)
                        cols = slice(s * B, (s + 1) * B)
                        dve.wait_ge(hc_ready, t + 1)
                        dve.wait_ge(gates_ready, t + 2)
                        v.tensor_tensor_scan(scan_flat(CC[:]), scan_flat(S[:, 0]), scan_flat(GC[:]), 0.0, ALU.mult, ALU.add).then_inc(cell_ready, 1)
                        dve.wait_ge(tanh_ready, t + 1)
                        v.scalar_tensor_tensor(out=h1[:], in0=S[:, 1, :, 1], scalar=SC, in1=tanh_c[:], op0=ALU.mult, op1=ALU.mult).then_inc(h1_ready, 1)
                        v.scalar_tensor_tensor(out=hs[k][:, cols], in0=S[:, 1, :, 1], scalar=SC, in1=tanh_c[:], op0=ALU.mult, op1=ALU.mult).then_inc(h32_ready, 1)
                        dve.wait_ge(h32_ready, t + 1)
                        v.tensor_tensor(h2[:], hs[k][:, cols], h1[:], ALU.subtract).then_inc(h2_ready, 1)
                        v.scalar_tensor_tensor(out=GC[:, :, 1], in0=hs[k][:, cols], scalar=1 / SC, in1=CC[:, :, 1], op0=ALU.mult, op1=ALU.mult).then_inc(hc_ready, 1)
                        fill(G, k, s, it)
            dve.wait_ge(hT_ps, NGRP + 1)
            dve.wait_ge(x2_stored, NGRP * 16 + 1)
            h_scaled_add(NGRP, 0)
            h_scaled_add(NGRP, 1).then_inc(x2_ready, 1)
            dve.wait_ge(x2_ready, NGRP + 1)
            for i in range(2):
                ins = v.bn_stats(st_y[:, i, :], x2s[:, i, :])
            link(ins)
            for i in range(2):
                ins = v.bn_aggr(mv_y[:, i, :], st_y[:, i, :])
            ins.then_inc(y_aggr, 1)
            dve.wait_ge(y_rstd, NGRP + 1)
            dve.wait_ge(y_stored, NGRP * 16 + 1)
            y_norm(NGRP)

            ROUTER_LINKS = 11

            def residual(f, par, fh):
                dve.wait_ge(cd_loaded[par], fh * 32 + 32)
                if not isinstance(f, int) or f >= 2:
                    dve.wait_ge(x3_copied, f - 1)
                dve.wait_ge(c_ps, f + 1)
                v.tensor_tensor(x3[par][:], PB[7][:].rearrange("p (b c d) -> p b c d", b=2, c=2),
                                x2r[par][:].rearrange("p c (b d) -> p b c d", b=2), ALU.add).then_inc(x3_ready, 1)

            def statistics(f, par):
                dve.wait_ge(x3_ready, f + 1)
                v.memset(tick_m[:], 0.0)
                for i in range(4):
                    ins = v.bn_stats(st_m[:, i, :], x3[par][:, i // 2, i % 2, :])
                ins.then_inc(m_stats, 1)
                dve.wait_ge(m_stats, f + 1)
                v.memset(tick_m[:], 0.0)
                for i in range(4):
                    ins = v.bn_aggr(mv_m[:, i, :], st_m[:, i, :])
                ins.then_inc(m_aggr, 1)

            def normalise(f, par):
                dve.wait_ge(m_rstd, f + 1)
                for i in range(4):
                    ins = v.tensor_scalar(xh[:, i, :], x3[par][:, i // 2, i % 2, :], mv_m[:, i, 0:1], rs_m[:, i:i + 1], ALU.subtract, ALU.mult)
                ins.then_inc(xh_ready, 1)

            def halves(f, par):
                dve.wait_ge(xhi_ready, f + 1)
                v.tensor_tensor(xlo[par][:], xnT[:], xhi[par][:].bitcast(F32), ALU.subtract).then_inc(xlo_ready, 1)

            def route(f, part):
                done = [0 if part == 0 else 4]

                def rlink(ins):
                    done[0] += 1
                    ins.then_inc(router_chain, 1)
                    dve.wait_ge(router_chain, f * ROUTER_LINKS + done[0])

                if part == 0:
                    dve.wait_ge(logits_ps, f + 1)
                    rlink(v.tensor_tensor(lg[:], PB[7][:, 0:4 * E].rearrange("p (i e) -> p i e", e=E), bc(br[:].unsqueeze(1), [P, 4, E]), ALU.add))
                    v.memset(tick_m[:], 0.0)
                    for i in range(4):
                        ins = v.max(top[:, i, :], lg[:, i, :])
                    rlink(ins)
                    v.tensor_tensor(dif[:], top[:, :, 0], top[:, :, 1], ALU.subtract).then_inc(dif_ready, 1)
                    for i in range(4):
                        ins = v.max_index(top_i[:, i, :], top[:, i, :], lg[:, i, :])
                    rlink(ins)
                    v.memset(tick_m[:], 0.0)
                    rlink(v.tensor_copy(idx[:], top_i[:, :, 0:2]))
                    v.tensor_tensor(oneh[:], bc(iota8.unsqueeze(1).unsqueeze(1), [P, 4, 2, E]), bc(idx[:].unsqueeze(3), [P, 4, 2, E]), ALU.is_equal)
                else:
                    dve.wait_ge(th_ready, f + 1)
                    v.tensor_scalar(w12[:, :, 0], th[:], 0.5, 0.5, ALU.mult, ALU.add)
                    rlink(v.tensor_scalar(w12[:, :, 1], th[:], -0.5, 0.5, ALU.mult, ALU.add))
                    rlink(v.tensor_tensor(ohw[:], oneh[:], bc(w12[:].unsqueeze(3), [P, 4, 2, E]), ALU.mult))
                    rlink(v.tensor_tensor(wf[:], ohw[:, :, 0, :], ohw[:, :, 1, :], ALU.add))
                    rlink(v.tensor_copy(wp[:, :, 0, :], wf[:]))
                    rlink(v.tensor_tensor(wra[:], wf[:], wp[:, :, 0, :], ALU.subtract))
                    rlink(v.tensor_copy(wp[:, :, 1, :], wra[:]))
                    rlink(v.tensor_tensor(wrb[:], wra[:], wp[:, :, 1, :], ALU.subtract))
                    v.tensor_copy(wp[:, :, 2, :], wrb[:]).then_inc(wp_ready, 1)

            def weighted(n, e, ring):
                if ring:
                    dve.wait_ge(glo_ready, n - 1)
                dve.wait_ge(wbc_ps, n + 1)
                dve.wait_ge(gelu_ready, n + 1)
                v.tensor_tensor(Gw[e % 2][:], Gl[e % 2][:], bc(PB[5][:].unsqueeze(1), [P, 2, 4 * P]), ALU.mult).then_inc(gw_ready, 1)

            def lower_half(n, e):
                dve.wait_ge(ghi_ready, n + 1)
                v.tensor_tensor(glo[e % 4][:], Gw[e % 2][:], ghi[e % 4][:].bitcast(F32), ALU.subtract).then_inc(glo_ready, 1)

            def out_add(o, par, oh):
                dve.wait_ge(x3_copied, o + 1)
                dve.wait_ge(yo_ps, o + 1)
                v.tensor_tensor(outb[par][:], PB[7][:].rearrange("p (b c d) -> p b c d", b=2, c=2), outb[par][:], ALU.add).then_inc(out_ready, 1)

            residual(0, 0, 0)
            statistics(0, 0)
            normalise(0, 0)
            halves(0, 0)
            route(0, 0)
            route(0, 1)

            def iteration(j, par, h):
                first, last = (isinstance(j, int) and j == q for q in (0, NB2 - 1))
                f, fpar = j + 1, 1 - par
                for e in range(E):
                    n = j * E + e
                    weighted(n, e, not (first and e < 2))
                    if not (first and e < 1):
                        lower_half(n - 1, (e - 1) % E)
                    if e == 3 and not first:
                        out_add(j - 1, 1 - par, h if par else h - 1)
                    if not last:
                        if e == 1:
                            residual(f, fpar, h + par)
                            statistics(f, fpar)
                        if e == 2:
                            normalise(f, fpar)
                        if e == 3:
                            halves(f, fpar)
                        if e == 4:
                            route(f, 0)
                        if e == 5:
                            route(f, 1)

            iterations(dve, iteration)
            lower_half(NB2 * E - 1, E - 1)
            out_add(NB2 - 1, 1, NB2 // 2 - 1)


def constants():
    import numpy as np

    c = np.zeros((P, C_N), np.float32)
    c[:, C_ID:C_ID + P] = np.eye(P)
    for g, nodes in enumerate(GROUPS):
        for j, n in enumerate(nodes):
            c[n, C_SEL + OFF[g] + j] = 1
            c[n, C_M5 + g] = 1
            for b in range(2):
                row = b * NP + OFF[g] + j
                c[row, C_MASK + b * NP + OFF[g]:C_MASK + b * NP + OFF[g + 1]] = 1
    c[:, C_IOTA:C_IOTA + E] = np.arange(E)
    c[:, C_ONES:C_ONES + P] = 1
    for p in range(3):
        for e in range(E):
            c[p * E + e, C_SELE + e * P:C_SELE + (e + 1) * P] = 1
    return c


_INS = ["x", "adj", "L0_gnn_W1", "L0_gnn_b1", "L0_gnn_W2", "L0_gnn_b2", "L0_gnn_fusion_w",
        "L0_ffn_U_i", "L0_ffn_V_i", "L0_ffn_b_i", "L0_ffn_U_c", "L0_ffn_V_c", "L0_ffn_b_c",
        "L0_ffn_U_o", "L0_ffn_V_o", "L0_ffn_b_o", "L1_gnn_W", "L1_gnn_b", "L1_gnn_alpha",
        "L1_ffn_gamma", "L1_ffn_beta", "L1_ffn_Wr", "L1_ffn_br", "L1_ffn_W1", "L1_ffn_b1", "L1_ffn_W2", "L1_ffn_b2"]


def kernel(**inputs):
    import numpy as np
    import concourse.bacc as bacc
    from concourse.bass_utils import run_bass_kernel_spmd

    nc = bacc.Bacc("TRN2", target_bir_lowering=False, num_devices=1)
    arrays = {f"in_{n}": np.ascontiguousarray(inputs[n]) for n in _INS}
    arrays["in_consts"] = constants()
    io = {n[3:]: nc.dram_tensor(n, a.shape, F32, kind="ExternalInput").ap() for n, a in arrays.items()}
    io["out"] = nc.dram_tensor("out", (B, T, D), F32, kind="ExternalOutput").ap()
    build(nc, io)
    return run_bass_kernel_spmd(nc, [arrays], core_ids=[0]).results[0]["out"]
```
